# Optimizing a Trainium2 kernel written in Bass

```python
import numpy as np
import jax
import jax.numpy as jnp

def _softmax(x, axis=-1):
    return jax.nn.softmax(x, axis=axis)

def _gelu(x):
    return jax.nn.gelu(x, approximate=True)

def _silu(x):
    return jax.nn.silu(x)

def _sigmoid(x):
    return jax.nn.sigmoid(x)

def _layernorm(x, axis=-1, eps=1e-05):
    m = jnp.mean(x, axis=axis, keepdims=True)
    v = jnp.var(x, axis=axis, keepdims=True)
    return (x - m) / jnp.sqrt(v + eps)

def _scatter_add(tgt, idx, src, axis=0):
    return tgt.at[idx].add(src)

def _segment_sum(src, seg, n):
    return jax.ops.segment_sum(src, seg, n)
kernel_name = 'mk_sandwich_d1_jaxref_r8_f00c97'

def setup_inputs(seed: int=0):
    np.random.seed(seed)
    _w = jnp.asarray

    def _L0_attn_setup():
        import jax, jax.numpy as jnp
        import numpy as np
        B, N, E = (4, 512, 256)
        H_DIM = 256
        HEADS = 16
        DH = H_DIM // HEADS
        LN_EPS = 1e-05

        def _heads(t):
            b, n, _ = t.shape
            return t.reshape(b, n, HEADS, DH).transpose(0, 2, 1, 3)

        def _layernorm(x, g, b):
            mu = jnp.mean(x, axis=-1, keepdims=True)
            var = jnp.mean(jnp.square(x - mu), axis=-1, keepdims=True)
            return (x - mu) * jax.lax.rsqrt(var + LN_EPS) * g + b
        key = jax.random.key(seed)
        ks = jax.random.split(key, 10)
        s = 1.0 / np.sqrt(E)
        so = 1.0 / np.sqrt(H_DIM)
        return {'x': jax.random.normal(ks[0], (B, N, E), jnp.float32), 'Wqk': jax.random.normal(ks[1], (E, H_DIM), jnp.float32) * s, 'bqk': jnp.zeros((H_DIM,), jnp.float32), 'Wv': jax.random.normal(ks[2], (E, H_DIM), jnp.float32) * s, 'bv': jnp.zeros((H_DIM,), jnp.float32), 'Wu': jax.random.normal(ks[3], (E, H_DIM), jnp.float32) * s, 'bu': jnp.zeros((H_DIM,), jnp.float32), 'Wo': jax.random.normal(ks[4], (H_DIM, E), jnp.float32) * so, 'bo': jnp.zeros((E,), jnp.float32), 'ln_g': jnp.ones((H_DIM,), jnp.float32), 'ln_b': jnp.zeros((H_DIM,), jnp.float32)}
    _L0_attn_in = _L0_attn_setup()

    def _L0_ffn_setup():
        import jax, jax.numpy as jnp
        import numpy as np
        E, K = (16, 4)
        C, H = (256, 448)
        B, T = (2, 64)
        STD = 0.02
        key = jax.random.key(seed)
        ks = jax.random.split(key, 5)
        x = jax.random.normal(ks[0], (B, T, C), jnp.float32)
        W_up = jax.random.normal(ks[1], (E, H, C), jnp.float32) * STD
        W_gate = jax.random.normal(ks[2], (E, H, C), jnp.float32) * STD
        W_down = jax.random.normal(ks[3], (E, C, H), jnp.float32) * STD
        gate_inp = jax.random.normal(ks[4], (E, C), jnp.float32) * STD
        return {'x': x, 'W_up': W_up, 'W_gate': W_gate, 'W_down': W_down, 'gate_inp': gate_inp}
    _L0_ffn_in = _L0_ffn_setup()
    _d = {'L0_attn_x': _L0_attn_in['x'], 'L0_attn_Wqk': _L0_attn_in['Wqk'], 'L0_attn_bqk': _L0_attn_in['bqk'], 'L0_attn_Wv': _L0_attn_in['Wv'], 'L0_attn_bv': _L0_attn_in['bv'], 'L0_attn_Wu': _L0_attn_in['Wu'], 'L0_attn_bu': _L0_attn_in['bu'], 'L0_attn_Wo': _L0_attn_in['Wo'], 'L0_attn_bo': _L0_attn_in['bo'], 'L0_attn_ln_g': _L0_attn_in['ln_g'], 'L0_attn_ln_b': _L0_attn_in['ln_b'], 'L0_ffn_W_up': _L0_ffn_in['W_up'], 'L0_ffn_W_gate': _L0_ffn_in['W_gate'], 'L0_ffn_W_down': _L0_ffn_in['W_down'], 'L0_ffn_gate_inp': _L0_ffn_in['gate_inp']}
    _x0 = _d['L0_attn_x']
    _d['L0_attn_x'] = jax.random.normal(jax.random.fold_in(jax.random.key(seed), 1), (4, 256, 256), dtype=_x0.dtype)
    del _x0
    return _d

def reference(L0_attn_x, L0_attn_Wqk, L0_attn_bqk, L0_attn_Wv, L0_attn_bv, L0_attn_Wu, L0_attn_bu, L0_attn_Wo, L0_attn_bo, L0_attn_ln_g, L0_attn_ln_b, L0_ffn_W_up, L0_ffn_W_gate, L0_ffn_W_down, L0_ffn_gate_inp):

    def _L0_attn_ref(x, Wqk, bqk, Wv, bv, Wu, bu, Wo, bo, ln_g, ln_b):
        import jax, jax.numpy as jnp
        import numpy as np
        B, N, E = (4, 512, 256)
        H_DIM = 256
        HEADS = 16
        DH = H_DIM // HEADS
        LN_EPS = 1e-05

        def _heads(t):
            b, n, _ = t.shape
            return t.reshape(b, n, HEADS, DH).transpose(0, 2, 1, 3)

        def _layernorm(x, g, b):
            mu = jnp.mean(x, axis=-1, keepdims=True)
            var = jnp.mean(jnp.square(x - mu), axis=-1, keepdims=True)
            return (x - mu) * jax.lax.rsqrt(var + LN_EPS) * g + b
        q = x @ Wqk + bqk
        k = x @ Wqk + bqk
        v = jax.nn.silu(x @ Wv + bv)
        u = jax.nn.silu(x @ Wu + bu)
        q = jax.nn.elu(_heads(q))
        kh = jax.nn.elu(_heads(k))
        vh = _heads(v)
        kv = jnp.einsum('bhnd,bhne->bhde', kh, vh)
        out = jnp.einsum('bhnd,bhde->bhne', q, kv)
        out = out.transpose(0, 2, 1, 3).reshape(x.shape[0], x.shape[1], H_DIM)
        out = _layernorm(out, ln_g, ln_b)
        out = u * out
        return out @ Wo + bo

    def _L0_ffn_ref(x, W_up, W_gate, W_down, gate_inp):
        import jax, jax.numpy as jnp
        import numpy as np
        E, K = (16, 4)
        C, H = (256, 448)
        B, T = (2, 64)
        STD = 0.02
        b, t, c = x.shape
        xf = x.reshape(b * t, c)
        logits = xf @ gate_inp.T
        topv, topi = jax.lax.top_k(logits, K)
        w = jax.nn.softmax(topv.astype(jnp.float32), axis=-1).astype(x.dtype)
        n = xf.shape[0]
        dense_w = jnp.zeros((n, E), x.dtype).at[jnp.arange(n)[:, None], topi].set(w)
        u = jnp.einsum('nc,ehc->neh', xf, W_up)
        g = jnp.einsum('nc,ehc->neh', xf, W_gate)
        h = jax.nn.silu(g) * u
        y = jnp.einsum('neh,ech,ne->nc', h, W_down, dense_w)
        return y.reshape(b, t, c)
    x = L0_attn_x
    x = x + _layernorm(_L0_attn_ref(_layernorm(x, axis=-1), L0_attn_Wqk, L0_attn_bqk, L0_attn_Wv, L0_attn_bv, L0_attn_Wu, L0_attn_bu, L0_attn_Wo, L0_attn_bo, L0_attn_ln_g, L0_attn_ln_b), axis=-1)
    x = x + _layernorm(_L0_ffn_ref(_layernorm(x, axis=-1), L0_ffn_W_up, L0_ffn_W_gate, L0_ffn_W_down, L0_ffn_gate_inp), axis=-1)
    return x

_drawn_inputs = setup_inputs


def setup_inputs(seed=0):
    import zlib

    import numpy as np

    out = dict(_drawn_inputs(seed))
    spreads = {'L0_attn_bqk': (0.0, 0.1),
     'L0_attn_bv': (0.0, 0.1),
     'L0_attn_bu': (0.0, 0.1),
     'L0_attn_bo': (0.0, 0.1),
     'L0_attn_ln_g': (1.0, 0.2),
     'L0_attn_ln_b': (0.0, 0.1)}
    factors = {}
    for name, (base, spread) in spreads.items():
        noise = np.random.default_rng([zlib.crc32(name.encode()), seed]).standard_normal(out[name].shape)
        drawn = base * np.exp(spread * noise) if base else spread * noise
        out[name] = jnp.asarray(drawn.astype(out[name].dtype))
    for name, factor in factors.items():
        out[name] = (out[name] * factor).astype(out[name].dtype)
    return out
```

```python
import concourse.bass as bass
from concourse import mybir
from contextlib import ExitStack

F32 = mybir.dt.float32
F32R = mybir.dt.float32r
F16 = mybir.dt.float16
I32 = mybir.dt.int32
ALU = mybir.AluOpType
ACT = mybir.ActivationFunctionType
AX = mybir.AxisListType


def sandwich_kernel(nc, x, wqk, bqk, wv, bv, wu, bu, wo, bo, ln_g, ln_b, w_ug, w_dn, gate_t, out):
    P = 128
    B, N, C = x.shape
    J = N // P
    KC = C // P
    W = J * C
    T = B * J
    TOK = B * N
    E, _, UGW = w_ug.shape
    HID = UGW // (2 * KC)
    _, HP, DNW = w_dn.shape
    HC = DNW // C
    K = 4
    HEAD = 16
    EPS = 1e-5
    RT = TOK // P + 1
    NT = (TOK * K + E * (P - 1)) // P + 1
    NB_RING = 4
    NB_RAW = 2
    WSCALE = 1024.0

    ctx = ExitStack()
    with ctx:
        def sb(name, shape, dt=F32):
            return ctx.enter_context(nc.sbuf_tensor(name, shape, dt))

        def sem(name):
            return ctx.enter_context(nc.semaphore(name))

        x_rows = nc.dram_tensor("x_rows", (TOK + P, C), F32, kind="Internal").ap()
        y_rows = nc.dram_tensor("y_rows", (TOK + P, C), F32, kind="Internal").ap()

        X = sb("X", [P, B, W])
        XN = sb("XN", [P, B, W])
        Q = sb("Q", [P, B, W])
        V = sb("V", [P, B, W])
        U = sb("U", [P, B, W])
        QT = sb("QT", [P, B, W])
        XT = sb("XT", [P, 2, W])
        wk = sb("wk", [P, 6, W])
        EXPQ, TV, TU = wk[:, 0:2, :], wk[:, 2:4, :], wk[:, 4:6, :]
        w_in = sb("w_in", [P, KC, 3 * C])
        w_out = sb("w_out", [P, KC, C])
        bias = sb("bias", [P, 3, C])
        bo_b = sb("bo_b", [P, C])
        g_b = sb("g_b", [P, C])
        b_b = sb("b_b", [P, C])
        gate_w = sb("gate_w", [P, KC, E])
        kvm = sb("kvm", [P, 2, C])
        ident = sb("ident", [P, P])
        blocks = sb("blocks", [P, P])
        before = sb("before", [P, P])
        ones = sb("ones", [P, P])
        st = sb("st", [P, T, 6])
        mv = sb("mv", [P, T, 2])
        rs = sb("rs", [P, T])
        nt1 = sb("nt1", [P, T])
        nt2 = sb("nt2", [P, T])
        raw_ug = sb("raw_ug", [P, NB_RAW, UGW])
        raw_dn = sb("raw_dn", [HP, NB_RAW, DNW])
        ug_hi = sb("ug_hi", [P, NB_RING, UGW], F32R)
        ug_lo = sb("ug_lo", [P, NB_RING, UGW], F32R)
        dn_hi = sb("dn_hi", [HP, NB_RING, DNW], F32R)
        dn_lo = sb("dn_lo", [HP, NB_RING, DNW], F32R)
        x_hi = sb("x_hi", [P, KC, P], F32R)
        x_lo = sb("x_lo", [P, KC, P], F32R)
        h_hi = sb("h_hi", [HP, HC, P], F32R)
        h_lo = sb("h_lo", [HP, HC, P], F32R)
        x_tile = wk[:, 0, 0:C]
        silu_g = wk[:, 1, 0:HID]
        h_tile = wk[:, 2, 0:HID]
        y_tile = wk[:, 3, 0:C]
        zero = wk[:, 5, 0:C]

        U_flat = U[:, :, :].rearrange("p b w -> p (b w)")

        def in_u(n, r, dt=F32):
            at = n * E * RT
            v = U_flat[:, at:at + E * r] if r == RT else U_flat[:, at:at + T * E]
            v = v if dt is F32 else v.bitcast(dt)
            return v.rearrange("p (e r) -> p e r", e=E) if r == RT else v.rearrange("p (t e) -> p t e", t=T)

        top = sb("top", [P, T, 8])
        topi = sb("topi", [P, T, 8], mybir.dt.uint32)
        idxf = sb("idxf", [P, T, K])
        ex = sb("ex", [P, T, K])
        exs = sb("exs", [P, T])
        lg = in_u(0, T)
        iota_e = sb("iota_e", [P, E])
        iota_r = sb("iota_r", [P, RT])
        iota_p = sb("iota_p", [P, P], F16)
        tok1 = sb("tok1", [P, T])
        spare = sb("spare", [P, 1])
        mask = sb("mask", [P, T, E])
        wsel = in_u(1, T)
        posi = in_u(5, T, I32)
        hi_i = in_u(4, T, I32)
        rowhi = in_u(3, T)
        rowlo = sb("rowlo", [P, T, E])
        cnt = sb("cnt", [P, E])
        ntl = sb("ntl", [P, E])
        tend = sb("tend", [P, E])
        onehot = QT[:, 0:1, :].rearrange("p b w -> p (b w)").rearrange("p (t k e) -> p t k e", t=T, k=K)
        onehot_w = QT[:, 1:2, :].rearrange("p b w -> p (b w)").rearrange("p (t k e) -> p t k e", t=T, k=K)
        hit = Q[:, 0:3, :].rearrange("p b w -> p (b w)")[:, 0:T * E * RT].rearrange(
            "p (t e r) -> p t e r", t=T, e=E)
        vals = XN[:, :, :].rearrange("p b w -> p (b w)").bitcast(F16)[:, 0:T * E * 3 * RT].rearrange(
            "p (t e q r) -> p t e q r", t=T, e=E, q=3)
        w_hi16 = sb("w_hi16", [P, T, E], F16)
        w_lo = in_u(2, T)
        sel = sb("sel", [P, 4, P], F16)
        inv_id = in_u(6, RT)
        inv_fix = in_u(7, RT)
        ids = sb("ids", [P, E * RT], I32)
        pair_w = sb("pair_w", [P, E, RT])
        gather_ids = sb("gather_ids", [P, 1], I32)
        scatter_ids = sb("scatter_ids", [P, 1], I32)
        iota_t = sb("iota_t", [1, NT])
        past = wk[0:1, 4, :]
        past = wk[0:1, 4:6, :].rearrange("o a w -> o (a w)")[:, 0:NT * (E - 1)].rearrange(
            "o (t e) -> o t e", t=NT)
        past_n = XT[0:1, :, :].rearrange("o a w -> o (a w)")[:, 0:NT * (E - 1)].rearrange(
            "o (t e) -> o t e", t=NT)
        tile_e = sb("tile_e", [1, NT + 1])
        tile_k = sb("tile_k", [1, NT])
        tile_new = sb("tile_new", [1, NT])
        tab_e = sb("tab_e", [1, NT], I32)
        tab_slot = sb("tab_slot", [1, NT], I32)
        tab_col = sb("tab_col", [1, NT], I32)
        tab_split = sb("tab_split", [1, NT], I32)

        bank = [ctx.enter_context(nc.psum_tensor(f"bank{i}", [P, 512], F32)) for i in range(8)]

        names = """x_loaded win_loaded bias_loaded wout_loaded lng_loaded gate_loaded raw_loaded
            zero_done rows_zeroed ident_done blocks_done const_done
            stats_done aggr_done newton xn_done xT_done xT_copied qk_done v_done u_done
            zq_done zv_done zu_done min_done exp_done tv_done tu_done q_ready v_ready u_ready
            qT_done qT_copied kv_done kv_masked out_done ln_scaled a1_done a2_done gated ouT_done ouT_copied
            wo_done y_biased yx_done x1_done nmr_done xn2_done rows_stored xn2T_done xn2T_copied logits_done
            lg_copied top_done topi_done idxf_done exin_done ex_done exs_done exr_done exw_done
            onehot_done mask_done ohw_done wsel_done prefix_done counts_done cnt_done r_chain
            hit_done vals_done sel_done sel_used inv_mm inv_done tables_done
            hi_split lo_split gather_id_ready gathered scatter_id_ready scattered
            tT_done t_hi t_lo gate_done up_done silu_done h_done hT_done hT_hi hT_lo down_done y_ready
            y_loaded f_chain f_ready out_stored""".split()
        S = {n: sem(n) for n in names}

        CH = sem("dve_chain")

        def first(t):
            return isinstance(t, int) and t == 0

        block = ctx.enter_context(nc.Block())

        @block.sync
        def _(sp):
            sp.dma_start(X[:, :, :].rearrange("p b (j c) -> p b j c", j=J),
                         x.rearrange("b (p j) c -> p b j c", j=J)).then_inc(S["x_loaded"], 16)
            for n, w in enumerate((wqk, wv, wu)):
                sp.dma_start(w_in[:, :, n * C:(n + 1) * C], w.rearrange("(k p) n -> p k n", p=P)).then_inc(
                    S["win_loaded"], 16)
            for n, v in enumerate((bqk, bv, bu)):
                sp.dma_start(bias[:, n, :], v.rearrange("(o n) -> o n", o=1).to_broadcast([P, C])).then_inc(
                    S["bias_loaded"], 16)
            sp.dma_start(w_out[:, :, :], wo.rearrange("(k p) n -> p k n", p=P)).then_inc(S["wout_loaded"], 16)
            for t, v in ((bo_b, bo), (g_b, ln_g), (b_b, ln_b)):
                sp.dma_start(t[:, :], v.rearrange("(o n) -> o n", o=1).to_broadcast([P, C])).then_inc(
                    S["lng_loaded"], 16)
            sp.dma_start(gate_w[:, :, :], gate_t.rearrange("(k p) n -> p k n", p=P)).then_inc(
                S["gate_loaded"], 16)
            sp.wait_ge(S["zero_done"], 1)
            sp.dma_start(y_rows.rearrange("(a p) c -> p a c", p=P),
                         zero.rearrange("p (a c) -> p a c", a=1).to_broadcast([P, T + 1, C])).then_inc(
                S["rows_zeroed"], 16)
            sp.dma_start(x_rows[TOK:TOK + P, :], zero).then_inc(S["rows_zeroed"], 16)

            def load_expert(e, slot):
                sp.dma_start(raw_ug[:, slot, :], w_ug[e, :, :]).then_inc(S["raw_loaded"], 16)
                sp.dma_start(raw_dn[:, slot, :], w_dn[e, :, :]).then_inc(S["raw_loaded"], 16)

            load_expert(0, 0)
            sp.wait_ge(S["raw_loaded"], 32)
            load_expert(1, 1)
            sp.wait_ge(S["raw_loaded"], 64)
            sp.wait_ge(S["lo_split"], 2)
            load_expert(2, 0)
            for b in range(B):
                sp.wait_ge(S["xn2_done"], J * (b + 1))
                sp.dma_start(x_rows[b * N:(b + 1) * N, :].rearrange("(p j) c -> p (j c)", j=J),
                             V[:, b, :]).then_inc(S["rows_stored"], 16)
            sp.wait_ge(S["raw_loaded"], 96)
            sp.wait_ge(S["lo_split"], 4)
            load_expert(3, 1)
            with sp.Fori(2, E // NB_RAW, 1) as pair:
                for slot in range(NB_RAW):
                    e = pair * NB_RAW + slot
                    sp.wait_ge(S["raw_loaded"], e * 32)
                    sp.wait_ge(S["lo_split"], e * 2 - 2)
                    load_expert(e, slot)
            sp.wait_ge(S["scattered"], 16 * (NT - 1))
            for b in range(B):
                sp.dma_start(Q[:, b, :], y_rows[b * N:(b + 1) * N, :].rearrange(
                    "(p j) c -> p (j c)", j=J)).then_inc(S["y_loaded"], 16)
            sp.wait_ge(S["rows_stored"], 16 * B)
            for b in range(B):
                sp.wait_ge(S["f_ready"], J * (b + 1))
                sp.dma_start(out[b].rearrange("(p j) c -> p (j c)", j=J), XN[:, b, :]).then_inc(
                    S["out_stored"], 16)
            sp.wait_ge(S["out_stored"], 16 * B)

        @block.gpsimd
        def _(pool):
            pool.memset(zero, 0.0).then_inc(S["zero_done"], 1)
            pool.memset(ident[:, :], 0.0).then_inc(S["ident_done"], 1)
            pool.memset(blocks[:, :], 0.5).then_inc(S["blocks_done"], 1)
            pool.memset(before[:, :], 1.0).then_inc(S["const_done"], 1)
            pool.memset(ones[:, :], 1.0).then_inc(S["const_done"], 1)
            pool.wait_ge(S["ident_done"], 1)
            pool.affine_select(out=ident[:, :], in_=ident[:, :], compare_op=ALU.not_equal, fill=1.0,
                               base=0, pattern=[[-1, P]], channel_multiplier=1).then_inc(S["ident_done"], 1)
            bl = blocks[:, :].rearrange("p (h d) -> p h d", d=HEAD)
            pool.wait_ge(S["blocks_done"], 1)
            pool.affine_select(out=bl, in_=bl, compare_op=ALU.is_ge, fill=0.0, base=0,
                               pattern=[[-HEAD, P // HEAD], [0, HEAD]], channel_multiplier=1).then_inc(
                S["blocks_done"], 1)
            pool.wait_ge(S["blocks_done"], 2)
            pool.affine_select(out=bl, in_=bl, compare_op=ALU.is_ge, fill=0.0, base=HEAD - 1,
                               pattern=[[HEAD, P // HEAD], [0, HEAD]], channel_multiplier=-1).then_inc(
                S["blocks_done"], 1)
            pool.wait_ge(S["const_done"], 1)
            pool.affine_select(out=before[:, :], in_=before[:, :], compare_op=ALU.is_ge, fill=0.0,
                               base=-1, pattern=[[1, P]], channel_multiplier=-1).then_inc(S["const_done"], 1)
            kw = dict(allow_small_or_imprecise_dtypes=True)
            pool.iota(iota_e[:, :], pattern=[[1, E]], base=0, channel_multiplier=0, **kw).then_inc(S["const_done"], 1)
            pool.iota(iota_r[:, :], pattern=[[1, RT]], base=0, channel_multiplier=0, **kw).then_inc(S["const_done"], 1)
            pool.iota(iota_p[:, :], pattern=[[1, P]], base=0, channel_multiplier=0, **kw).then_inc(S["const_done"], 1)
            pool.iota(iota_t[:, :], pattern=[[1, NT]], base=0, channel_multiplier=0, **kw).then_inc(S["const_done"], 1)
            pool.iota(tok1[:, :].rearrange("p (b j) -> p b j", j=J), pattern=[[N, B], [1, J]], base=1,
                      channel_multiplier=J, **kw).then_inc(S["const_done"], 1)
            pool.iota(spare[:, :], pattern=[[0, 1]], base=TOK + 1, channel_multiplier=1, **kw).then_inc(
                S["const_done"], 1)
            pool.wait_ge(S["rows_zeroed"], 32)
            for b in range(B):
                pool.wait_ge(S["tu_done"], b + 1)
                pool.tensor_tensor(TU[:, b % 2, :], TU[:, b % 2, :], U[:, b, :], ALU.mult).then_inc(S["r_chain"], 1)
                pool.wait_ge(S["r_chain"], b + 1)
                pool.tensor_tensor(U[:, b, :], TU[:, b % 2, :], U[:, b, :], ALU.add).then_inc(S["u_ready"], 1)

            for e in range(NB_RING - 1):
                pool.wait_ge(S["hi_split"], 2 * e + 2)
                pool.tensor_tensor(ug_lo[:, e, :], raw_ug[:, e % NB_RAW, :], ug_hi[:, e, :].bitcast(F32),
                                   ALU.subtract).then_inc(S["lo_split"], 1)
                pool.tensor_tensor(dn_lo[:, e, :], raw_dn[:, e % NB_RAW, :], dn_hi[:, e, :].bitcast(F32),
                                   ALU.subtract).then_inc(S["lo_split"], 1)

            def take_ids(dst, t):
                col = pool.value_load(tab_col[0:1, bass.ds(t, 1)], min_val=0, max_val=E * RT - 1)
                return pool.tensor_copy(dst[:, :], ids[:, bass.ds(col, 1)])

            def gather(t, before_copy=None):
                take_ids(gather_ids, t).then_inc(S["gather_id_ready"], 1)
                pool.wait_ge(S["gather_id_ready"], 1)
                pool.indirect_dma_start(x_tile, None, x_rows[:, :],
                                        bass.IndirectOffsetOnAxis(ap=gather_ids[:, 0:1], axis=0)).then_inc(
                    S["gathered"], 16)
                pool.sem_clear(S["gather_id_ready"])

            def scatter(t):
                if not first(t):
                    pool.wait_ge(S["scattered"], t * 16)
                pool.wait_ge(S["y_ready"], t + 1)
                take_ids(scatter_ids, t).then_inc(S["scatter_id_ready"], 1)
                pool.wait_ge(S["scatter_id_ready"], 1)
                pool.indirect_dma_start(y_rows[:, :],
                                        bass.IndirectOffsetOnAxis(ap=scatter_ids[:, 0:1], axis=0),
                                        y_tile, None, compute_op=ALU.add).then_inc(S["scattered"], 16)
                pool.sem_clear(S["scatter_id_ready"])

            pool.wait_ge(S["tables_done"], 1)
            pool.wait_ge(S["inv_done"], 1)
            pool.wait_ge(S["rows_stored"], 16 * B)
            gather(0)
            pool.wait_ge(S["tT_done"], 1)
            pool.wait_ge(S["gathered"], 16)
            gather(1)

            def step(t):
                pool.wait_ge(S["tT_done"], t + 2)
                pool.wait_ge(S["gathered"], (t + 2) * 16)
                gather(t + 2)
                scatter(t)

            step(0)
            with pool.Fori(1, NT - 2, 1) as t:
                step(t)
            scatter(NT - 2)
            pool.wait_ge(S["gathered"], NT * 16)
            pool.wait_ge(S["scattered"], (NT - 1) * 16)

        @block.vector
        def _(dve):
            count = {"newton": 0, "aggr_done": 0, "r": 0, "stats": 0}

            def link(ins):
                count["r"] += 1
                ins.then_inc(CH, 1)
                dve.wait_ge(CH, count["r"])

            def stats(tile, i):
                count["stats"] += 1
                dve.bn_stats(st[:, i, :], tile).then_inc(S["stats_done"], 1)

            def rstd_of_all():
                dve.wait_ge(S["stats_done"], count["stats"])
                for i in range(T):
                    last = dve.bn_aggr(mv[:, i, :], st[:, i, :])
                link(last)
                v = nt1[:, :]
                link(dve.tensor_scalar(v, mv[:, :, 1], EPS, None, ALU.add))
                link(dve.tensor_scalar(nt2[:, :].bitcast(I32), v.bitcast(I32), 1, None, ALU.logical_shift_right))
                link(dve.tensor_scalar(rs[:, :].bitcast(I32), nt2[:, :].bitcast(I32), -1.0, float(0x5F3759DF),
                                       ALU.mult, ALU.add))
                for _ in range(3):
                    link(dve.scalar_tensor_tensor(out=nt2[:, :], in0=rs[:, :], scalar=-0.5, in1=rs[:, :],
                                                  op0=ALU.mult, op1=ALU.mult))
                    link(dve.tensor_tensor(nt2[:, :], nt2[:, :], v, ALU.mult))
                    link(dve.scalar_tensor_tensor(out=rs[:, :], in0=nt2[:, :], scalar=1.5, in1=rs[:, :],
                                                  op0=ALU.add, op1=ALU.mult))

            def slot(t, b, j):
                return t[:, b, j * C:(j + 1) * C]

            def wide(t):
                return t.rearrange("p (j c) -> p j c", j=J)

            def over_slots(v):
                return v.rearrange("p (o c) -> p o c", o=1).to_broadcast([P, J, C])

            dve.wait_ge(S["x_loaded"], 16)
            for b in range(B):
                for j in range(J):
                    stats(slot(X, b, j), b * J + j)
            rstd_of_all()
            for b in range(B):
                for j in range(J):
                    i = b * J + j
                    dve.tensor_scalar(slot(XN, b, j), slot(X, b, j), mv[:, i, 0:1], rs[:, i:i + 1],
                                      ALU.subtract, ALU.mult).then_inc(S["xn_done"], 1)

            dve.wait_ge(S["bias_loaded"], 48)
            for s in range(B + 1):
                if s < B:
                    b = s
                    for n, (dst, ps, ready, done) in enumerate((
                            (Q, bank[b % 2], "qk_done", "zq_done"), (V, bank[2 + b % 2], "v_done", "zv_done"),
                            (U, bank[4 + b % 2], "u_done", "zu_done"))):
                        dve.wait_ge(S[ready], b + 1)
                        dve.tensor_tensor(wide(dst[:, b, :]), wide(ps[:, :]), over_slots(bias[:, n, :]),
                                          ALU.add).then_inc(S[done], 1)
                    dve.wait_ge(S["zq_done"], b + 1)
                    if b >= 2:
                        dve.wait_ge(S["q_ready"], b - 1)
                    dve.tensor_scalar(EXPQ[:, b % 2, :], Q[:, b, :], 0.0, None, ALU.min).then_inc(
                        S["min_done"], 1)
                if s >= 1:
                    b = s - 1
                    dve.wait_ge(S["exp_done"], b + 1)
                    dve.scalar_tensor_tensor(out=Q[:, b, :], in0=EXPQ[:, b % 2, :], scalar=-1.0, in1=Q[:, b, :],
                                             op0=ALU.add, op1=ALU.max).then_inc(S["q_ready"], 1)
                    dve.wait_ge(S["tv_done"], b + 1)
                    dve.scalar_tensor_tensor(out=V[:, b, :], in0=TV[:, b % 2, :], scalar=1.0, in1=V[:, b, :],
                                             op0=ALU.add, op1=ALU.mult).then_inc(S["v_ready"], 1)

            dve.wait_ge(S["lng_loaded"], 48)
            dve.tensor_scalar(g_b[:, :], g_b[:, :], 0.5, None, ALU.mult).then_inc(S["ln_scaled"], 1)
            dve.tensor_scalar(b_b[:, :], b_b[:, :], 0.5, None, ALU.mult).then_inc(S["ln_scaled"], 1)
            dve.wait_ge(S["blocks_done"], 3)
            for s in range(B + 1):
                if s < B:
                    b = s
                    dve.wait_ge(S["kv_done"], b + 1)
                    if b >= 2:
                        dve.wait_ge(S["out_done"], b - 1)
                    dve.tensor_tensor(kvm[:, b % 2, :].rearrange("p (k c) -> p k c", k=KC),
                                      bank[6 + b % 2][:, 0:C].rearrange("p (k c) -> p k c", k=KC),
                                      blocks[:, :].rearrange("p (o c) -> p o c", o=1).to_broadcast([P, KC, P]),
                                      ALU.mult).then_inc(S["kv_masked"], 1)
                if s >= 1:
                    b = s - 1
                    dve.wait_ge(S["out_done"], b + 1)
                    for j in range(J):
                        stats(bank[b][:, j * C:(j + 1) * C], b * J + j)
            rstd_of_all()
            dve.wait_ge(S["ln_scaled"], 2)
            for b in range(B):
                for j in range(J):
                    i = b * J + j
                    dve.scalar_tensor_tensor(out=slot(XN, b, j), in0=bank[b][:, j * C:(j + 1) * C],
                                             scalar=mv[:, i, 0:1], in1=g_b[:, :],
                                             op0=ALU.subtract, op1=ALU.mult).then_inc(S["a1_done"], 1)
                for j in range(J):
                    i = b * J + j
                    dve.wait_ge(S["a1_done"], i + 1)
                    dve.scalar_tensor_tensor(out=slot(XN, b, j), in0=slot(XN, b, j),
                                             scalar=rs[:, i:i + 1], in1=b_b[:, :],
                                             op0=ALU.mult, op1=ALU.add).then_inc(S["a2_done"], 1)
                dve.wait_ge(S["u_ready"], b + 1)
                dve.wait_ge(S["a2_done"], J * (b + 1))
                dve.tensor_tensor(XN[:, b, :], XN[:, b, :], U[:, b, :], ALU.mult).then_inc(S["gated"], 1)

            for b in range(B):
                dve.wait_ge(S["wo_done"], b + 1)
                dve.tensor_tensor(wide(Q[:, b, :]), wide(bank[6 + b % 2][:, :]), over_slots(bo_b[:, :]),
                                  ALU.add).then_inc(S["y_biased"], 1)
                dve.wait_ge(S["y_biased"], b + 1)
                for j in range(J):
                    stats(slot(Q, b, j), b * J + j)
            rstd_of_all()
            link(dve.scalar_tensor_tensor(out=nt1[:, :], in0=mv[:, :, 0], scalar=-1.0, in1=rs[:, :],
                                          op0=ALU.mult, op1=ALU.mult))
            for b in range(B):
                for j in range(J):
                    i = b * J + j
                    dve.scalar_tensor_tensor(out=slot(Q, b, j), in0=slot(Q, b, j), scalar=rs[:, i:i + 1],
                                             in1=slot(X, b, j), op0=ALU.mult, op1=ALU.add).then_inc(
                        S["yx_done"], 1)
            for b in range(B):
                for j in range(J):
                    i = b * J + j
                    dve.wait_ge(S["yx_done"], i + 1)
                    dve.tensor_scalar(slot(X, b, j), slot(Q, b, j), nt1[:, i:i + 1], None,
                                      ALU.add).then_inc(S["x1_done"], 1)
            for b in range(B):
                for j in range(J):
                    dve.wait_ge(S["x1_done"], b * J + j + 1)
                    stats(slot(X, b, j), b * J + j)
            rstd_of_all()
            for b in range(B):
                for j in range(J):
                    i = b * J + j
                    dve.tensor_scalar(slot(V, b, j), slot(X, b, j), mv[:, i, 0:1], rs[:, i:i + 1],
                                      ALU.subtract, ALU.mult).then_inc(S["xn2_done"], 1)

            dve.wait_ge(S["logits_done"], B)
            link(dve.tensor_copy(lg[:, :, :].rearrange("p t e -> p (t e)"), bank[2][:, 0:T * E]))
            for i in range(T):
                last = dve.max(top[:, i, :], lg[:, i, :])
            link(last)
            for i in range(T):
                last = dve.max_index(topi[:, i, :], top[:, i, :], lg[:, i, :])
            link(last)
            link(dve.tensor_copy(idxf[:, :, :], topi[:, :, 0:K]))
            dve.tensor_tensor(ex[:, :, :], top[:, :, 0:K], top[:, :, 0:1].to_broadcast([P, T, K]),
                              ALU.subtract).then_inc(S["exin_done"], 1)
            dve.wait_ge(S["const_done"], 9)
            link(dve.tensor_tensor(onehot, iota_e[:, :].rearrange("p (a b e) -> p a b e", a=1, b=1).to_broadcast(
                [P, T, K, E]), idxf[:, :, :].rearrange("p t (k o) -> p t k o", o=1).to_broadcast([P, T, K, E]),
                ALU.is_equal))
            dve.tensor_reduce(out=mask[:, :, :], in_=onehot.rearrange("p t k e -> p t e k"), op=ALU.add,
                              axis=AX.X).then_inc(S["mask_done"], 1)
            dve.wait_ge(S["ex_done"], 1)
            link(dve.tensor_reduce(out=exs[:, :], in_=ex[:, :, :], op=ALU.add, axis=AX.X))
            link(dve.reciprocal(exs[:, :], exs[:, :]))
            link(dve.scalar_tensor_tensor(out=ex[:, :, :], in0=ex[:, :, :], scalar=WSCALE,
                                          in1=exs[:, :].rearrange("p (t o) -> p t o", o=1).to_broadcast([P, T, K]),
                                          op0=ALU.mult, op1=ALU.mult))
            link(dve.tensor_tensor(onehot_w, onehot, ex[:, :, :].rearrange("p t (k o) -> p t k o", o=1).to_broadcast(
                [P, T, K, E]), ALU.mult))
            link(dve.tensor_reduce(out=wsel[:, :, :], in_=onehot_w.rearrange("p t k e -> p t e k"), op=ALU.add,
                                   axis=AX.X))
            link(dve.tensor_copy(w_hi16[:, :, :], wsel[:, :, :]))
            link(dve.tensor_tensor(w_lo[:, :, :], wsel[:, :, :], w_hi16[:, :, :], ALU.subtract))

            dve.wait_ge(S["prefix_done"], 1)
            flat = [t[:, :, :].rearrange("p t e -> p (t e)") for t in (posi, mask, hi_i, rowhi, rowlo)]
            posi_f, mask_f, hi_f, rowhi_f, rowlo_f = flat
            link(dve.scalar_tensor_tensor(out=rowlo_f, in0=bank[3][:, 0:T * E], scalar=1.0, in1=mask_f,
                                          op0=ALU.add, op1=ALU.mult))
            link(dve.tensor_scalar(posi_f, rowlo_f, -1.0, None, ALU.add))
            link(dve.tensor_scalar(hi_f, posi_f, 7, None, ALU.arith_shift_right))
            link(dve.tensor_scalar(posi_f, posi_f, P - 1, None, ALU.bitwise_and))
            dve.tensor_copy(rowlo_f, posi_f)
            link(dve.tensor_copy(rowhi_f, hi_f))
            link(dve.tensor_tensor(hit, iota_r[:, :].rearrange("p (a b r) -> p a b r", a=1, b=1).to_broadcast(
                [P, T, E, RT]), rowhi[:, :, :].rearrange("p t (e o) -> p t e o", o=1).to_broadcast([P, T, E, RT]),
                ALU.is_equal))
            dve.tensor_tensor(vals[:, :, :, 0, :], hit, tok1[:, :].rearrange(
                "p (t a b) -> p t a b", a=1, b=1).to_broadcast([P, T, E, RT]), ALU.mult)
            dve.tensor_tensor(vals[:, :, :, 1, :], hit, w_hi16[:, :, :].rearrange(
                "p t (e o) -> p t e o", o=1).to_broadcast([P, T, E, RT]), ALU.mult)
            dve.tensor_tensor(vals[:, :, :, 2, :], hit, w_lo[:, :, :].rearrange(
                "p t (e o) -> p t e o", o=1).to_broadcast([P, T, E, RT]), ALU.mult).then_inc(S["vals_done"], 1)

            dve.wait_ge(S["counts_done"], 1)
            link(dve.tensor_copy(cnt[:, :], bank[4][:, 0:E]))
            link(dve.tensor_scalar(ntl[:, :], cnt[:, :], float(P), 1.0, ALU.is_gt, ALU.add))
            for r in range(2, RT - 1):
                link(dve.scalar_tensor_tensor(out=ntl[:, :], in0=cnt[:, :], scalar=float(r * P), in1=ntl[:, :],
                                              op0=ALU.is_gt, op1=ALU.add))
            link(dve.tensor_tensor_scan(out=tend[:, :], data0=ones[:, 0:E], data1=ntl[:, :], initial=0.0,
                                        op0=ALU.mult, op1=ALU.add))
            link(dve.tensor_tensor(past, tend[0:1, 0:E - 1].rearrange("o (a e) -> o a e", a=1).to_broadcast(
                [1, NT, E - 1]), iota_t[:, :].rearrange("o (t a) -> o t a", a=1).to_broadcast([1, NT, E - 1]),
                ALU.is_le))
            link(dve.memset(tile_e[:, 0:1], -1.0))
            link(dve.tensor_reduce(out=tile_e[:, 1:NT + 1], in_=past, op=ALU.add, axis=AX.X))
            link(dve.tensor_tensor(past_n, past, ntl[0:1, 0:E - 1].rearrange("o (a e) -> o a e", a=1).to_broadcast(
                [1, NT, E - 1]), ALU.mult))
            link(dve.tensor_reduce(out=tile_k[:, :], in_=past_n, op=ALU.add, axis=AX.X))
            link(dve.tensor_tensor(tile_k[:, :], iota_t[:, :], tile_k[:, :], ALU.subtract))
            link(dve.tensor_scalar(tile_k[:, :], tile_k[:, :], float(RT - 1), None, ALU.min))
            link(dve.scalar_tensor_tensor(out=tab_col[:, :], in0=tile_e[:, 1:NT + 1], scalar=float(RT),
                                          in1=tile_k[:, :], op0=ALU.mult, op1=ALU.add))
            link(dve.tensor_copy(tab_e[:, :], tile_e[:, 1:NT + 1]))
            link(dve.tensor_scalar(tab_slot[:, :], tab_e[:, :], NB_RING - 1, None, ALU.bitwise_and))
            link(dve.tensor_tensor(tile_new[:, :], tile_e[:, 1:NT + 1], tile_e[:, 0:NT], ALU.is_equal))
            link(dve.tensor_scalar(tile_new[:, :], tile_new[:, :], float(E), float(NB_RING - 1),
                                   ALU.mult, ALU.add))
            dve.tensor_tensor(tab_split[:, :], tile_new[:, :], tile_e[:, 1:NT + 1], ALU.add).then_inc(
                S["tables_done"], 1)

            n = 0
            for e in range(E):
                for i in range(T):
                    if n >= 4:
                        dve.wait_ge(S["sel_used"], n - 3)
                    dve.tensor_scalar(sel[:, n % 4, :], iota_p[:, :], rowlo[:, i, e:e + 1], None,
                                      ALU.is_equal).then_inc(S["sel_done"], 1)
                    n += 1
            dve.wait_ge(S["inv_mm"], 1)
            inv = bank[5][:, 0:E * 3 * RT].rearrange("p (e q r) -> p e q r", e=E, q=3)
            link(dve.tensor_copy(inv_id[:, :, :], inv[:, :, 0, :]))
            link(dve.tensor_scalar(inv_fix[:, :, :], inv_id[:, :, :], 0.5, spare[:, 0:1], ALU.is_lt, ALU.mult))
            link(dve.scalar_tensor_tensor(out=ids[:, :].rearrange("p (e r) -> p e r", e=E), in0=inv_id[:, :, :],
                                          scalar=-1.0, in1=inv_fix[:, :, :], op0=ALU.add, op1=ALU.add))
            link(dve.tensor_scalar(inv_fix[:, :, :], inv[:, :, 1, :], 1.0 / WSCALE, None, ALU.mult))
            dve.scalar_tensor_tensor(out=pair_w[:, :, :], in0=inv[:, :, 2, :], scalar=1.0 / WSCALE,
                                     in1=inv_fix[:, :, :], op0=ALU.mult, op1=ALU.add).then_inc(S["inv_done"], 1)

            def x_low(t):
                dve.wait_ge(S["t_hi"], t + 1)
                dve.tensor_tensor(x_lo[:, :, :], bank[3][:, 0:C].rearrange("p (k c) -> p k c", k=KC),
                                  x_hi[:, :, :].bitcast(F32), ALU.subtract).then_inc(S["t_lo"], 1)

            def hidden(t):
                dve.wait_ge(S["silu_done"], t + 1)
                dve.wait_ge(S["up_done"], t + 1)
                dve.tensor_tensor(h_tile, silu_g, bank[1][:, 0:HID], ALU.mult).then_inc(S["h_done"], 1)

            def h_low(t):
                dve.wait_ge(S["hT_hi"], t + 1)
                dve.tensor_tensor(h_lo[:, :, :], bank[2][0:HP, :].rearrange("p (k c) -> p k c", k=HC),
                                  h_hi[:, :, :].bitcast(F32), ALU.subtract).then_inc(S["hT_lo"], 1)

            def split_low(e, ring, raw, ready):
                dve.wait_ge(S["hi_split"], ready)
                dve.tensor_tensor(ug_lo[:, ring, :], raw_ug[:, raw, :], ug_hi[:, ring, :].bitcast(F32),
                                  ALU.subtract).then_inc(S["lo_split"], 1)
                dve.tensor_tensor(dn_lo[:, ring, :], raw_dn[:, raw, :], dn_hi[:, ring, :].bitcast(F32),
                                  ALU.subtract).then_inc(S["lo_split"], 1)

            x_low(0)
            hidden(0)
            x_low(1)

            def step(t):
                h_low(t)
                hidden(t + 1)
                x_low(t + 2)
                e = dve.value_load(tab_split[0:1, bass.ds(t, 1)], min_val=0, max_val=3 * E)
                with dve.If(e < E):
                    split_low(e, dve.snap(e & (NB_RING - 1)), dve.snap(e & (NB_RAW - 1)), 2 * e + 2)

            step(0)
            with dve.Fori(1, NT - 2, 1) as t:
                step(t)
            h_low(NT - 2)

            dve.wait_ge(S["y_loaded"], 16 * B)
            for b in range(B):
                for j in range(J):
                    stats(slot(Q, b, j), b * J + j)
            rstd_of_all()
            link(dve.scalar_tensor_tensor(out=nt1[:, :], in0=mv[:, :, 0], scalar=-1.0, in1=rs[:, :],
                                          op0=ALU.mult, op1=ALU.mult))
            for b in range(B):
                for j in range(J):
                    i = b * J + j
                    dve.scalar_tensor_tensor(out=slot(Q, b, j), in0=slot(Q, b, j), scalar=rs[:, i:i + 1],
                                             in1=slot(X, b, j), op0=ALU.mult, op1=ALU.add).then_inc(
                        S["f_chain"], 1)
                for j in range(J):
                    i = b * J + j
                    dve.wait_ge(S["f_chain"], i + 1)
                    dve.tensor_scalar(slot(XN, b, j), slot(Q, b, j), nt1[:, i:i + 1], None,
                                      ALU.add).then_inc(S["f_ready"], 1)

        @block.scalar
        def _(act):
            def split_high(ring, raw, loaded):
                act.wait_ge(S["raw_loaded"], loaded)
                act.activation(ug_hi[:, ring, :], raw_ug[:, raw, :], ACT.Copy).then_inc(S["hi_split"], 1)
                act.activation(dn_hi[:, ring, :], raw_dn[:, raw, :], ACT.Copy).then_inc(S["hi_split"], 1)

            for s in range(B + 2):
                if s < B:
                    b = s
                    act.wait_ge(S["xT_done"], b + 1)
                    if b >= 2:
                        act.wait_ge(S["u_done"], b - 1)
                    act.copy(XT[:, b % 2, :], bank[6][:, :]).then_inc(S["xT_copied"], 1)
                if 0 <= s - 1 < B:
                    b = s - 1
                    act.wait_ge(S["min_done"], b + 1)
                    act.activation(EXPQ[:, b % 2, :], EXPQ[:, b % 2, :], ACT.Exp).then_inc(S["exp_done"], 1)
                    act.wait_ge(S["zv_done"], b + 1)
                    if b >= 2:
                        act.wait_ge(S["v_ready"], b - 1)
                    act.activation(TV[:, b % 2, :], V[:, b, :], ACT.Tanh, scale=0.5).then_inc(S["tv_done"], 1)
                    act.wait_ge(S["zu_done"], b + 1)
                    if b >= 2:
                        act.wait_ge(S["u_ready"], b - 1)
                    if b == 0:
                        act.wait_ge(S["rows_zeroed"], 32)
                    act.activation(TU[:, b % 2, :], U[:, b, :], ACT.Tanh, scale=0.5).then_inc(S["tu_done"], 1)
                if s >= 2:
                    b = s - 2
                    act.wait_ge(S["qT_done"], b + 1)
                    act.copy(QT[:, b, :], bank[7][:, :]).then_inc(S["qT_copied"], 1)
            for e in range(2):
                split_high(e, e, 32 * (e + 1))
            for b in range(B):
                act.wait_ge(S["ouT_done"], b + 1)
                if b >= 2:
                    act.wait_ge(S["wo_done"], b - 1)
                act.copy(XT[:, b % 2, :], bank[4 + b % 2][:, :]).then_inc(S["ouT_copied"], 1)
            split_high(2, 0, 96)
            for b in range(B):
                act.wait_ge(S["xn2T_done"], b + 1)
                act.copy(QT[:, b, :], bank[b % 2][:, :]).then_inc(S["xn2T_copied"], 1)
            act.wait_ge(S["exin_done"], 1)
            act.activation(ex[:, :, :], ex[:, :, :], ACT.Exp).then_inc(S["ex_done"], 1)

            def x_high(t):
                act.wait_ge(S["tT_done"], t + 1)
                act.activation(x_hi[:, :, :], bank[3][:, 0:C].rearrange("p (k c) -> p k c", k=KC),
                               ACT.Copy).then_inc(S["t_hi"], 1)

            def silu(t):
                act.wait_ge(S["gate_done"], t + 1)
                act.activation(silu_g, bank[0][:, 0:HID], ACT.Silu).then_inc(S["silu_done"], 1)

            def h_high(t):
                act.wait_ge(S["hT_done"], t + 1)
                act.activation(h_hi[:, :, :], bank[2][0:HP, :].rearrange("p (k c) -> p k c", k=HC),
                               ACT.Copy).then_inc(S["hT_hi"], 1)

            def y_out(t):
                col = act.value_load(tab_col[0:1, bass.ds(t, 1)], min_val=0, max_val=E * RT - 1)
                act.wait_ge(S["down_done"], t + 1)
                if not first(t):
                    act.wait_ge(S["scattered"], 16 * t)
                act.activation(y_tile, bank[4][:, 0:C], ACT.Copy,
                               scale=pair_w[:, :, :].rearrange("p e r -> p (e r)")[:, bass.ds(col, 1)]).then_inc(
                    S["y_ready"], 1)

            act.wait_ge(S["inv_done"], 1)
            x_high(0)
            silu(0)
            x_high(1)

            def step(t):
                act.wait_ge(S["h_done"], t + 1)
                silu(t + 1)
                h_high(t)
                x_high(t + 2)
                y_out(t)
                e = act.value_load(tab_split[0:1, bass.ds(t, 1)], min_val=0, max_val=3 * E)
                with act.If(e < E):
                    if not first(t):
                        act.wait_ge(S["down_done"], t)
                    split_high(act.snap(e & (NB_RING - 1)), act.snap(e & (NB_RAW - 1)), 32 * e + 32)

            step(0)
            with act.Fori(1, NT - 2, 1) as t:
                step(t)
            h_high(NT - 2)
            y_out(NT - 2)

        @block.tensor
        def _(pe):
            def transpose_batch(ps, src, done):
                for k in range(KC):
                    for j in range(J):
                        last = pe.transpose(ps[:, (k * J + j) * P:(k * J + j + 1) * P],
                                            src[:, j * C + k * P:j * C + (k + 1) * P], ident[:, :])
                last.then_inc(S[done], 1)

            def chunk(t, k, j):
                return t[:, (k * J + j) * P:(k * J + j + 1) * P]

            def project(ps, src, rhs, done):
                for j in range(J):
                    for k in range(KC):
                        last = pe.matmul(ps[:, j * C:(j + 1) * C], chunk(src, k, j), rhs[k],
                                         start=(k == 0), stop=(k == KC - 1))
                last.then_inc(S[done], 1)

            pe.wait_ge(S["ident_done"], 2)
            for s in range(B + 2):
                if s < B:
                    b = s
                    pe.wait_ge(S["xn_done"], J * (b + 1))
                    if b >= 1:
                        pe.wait_ge(S["xT_copied"], b)
                    transpose_batch(bank[6], XN[:, b, :], "xT_done")
                if 0 <= s - 1 < B:
                    b = s - 1
                    if b == 0:
                        pe.wait_ge(S["win_loaded"], 48)
                    pe.wait_ge(S["xT_copied"], b + 1)
                    for n, (done, free) in enumerate((("qk_done", "zq_done"), ("v_done", "zv_done"),
                                                      ("u_done", "zu_done"))):
                        if b >= 2:
                            pe.wait_ge(S[free], b - 1)
                        project(bank[2 * n + b % 2], XT[:, b % 2, :],
                                [w_in[:, k, n * C:(n + 1) * C] for k in range(KC)], done)
                if s >= 2:
                    b = s - 2
                    pe.wait_ge(S["q_ready"], b + 1)
                    if b >= 1:
                        pe.wait_ge(S["qT_copied"], b)
                    transpose_batch(bank[7], Q[:, b, :], "qT_done")

            pe.wait_ge(S["zu_done"], B)
            for s in range(B + 1):
                if s < B:
                    b = s
                    pe.wait_ge(S["v_ready"], b + 1)
                    if b == 1:
                        pe.wait_ge(S["qT_copied"], B)
                    if b >= 2:
                        pe.wait_ge(S["kv_masked"], b - 1)
                    for k in range(KC):
                        for j in range(J):
                            lo = j * C + k * P
                            last = pe.matmul(bank[6 + b % 2][:, k * P:(k + 1) * P], Q[:, b, lo:lo + P],
                                             V[:, b, lo:lo + P], start=(j == 0), stop=(j == J - 1))
                    last.then_inc(S["kv_done"], 1)
                if s >= 1:
                    b = s - 1
                    pe.wait_ge(S["kv_masked"], b + 1)
                    pe.wait_ge(S["qT_copied"], b + 1)
                    for j in range(J):
                        for k in range(KC):
                            last = pe.matmul(bank[b][:, j * C + k * P:j * C + (k + 1) * P],
                                             chunk(QT[:, b, :], k, j), kvm[:, b % 2, k * P:(k + 1) * P],
                                             start=True, stop=True)
                    last.then_inc(S["out_done"], 1)

            pe.wait_ge(S["wout_loaded"], 16)
            for s in range(B + 1):
                if s < B:
                    b = s
                    pe.wait_ge(S["gated"], b + 1)
                    if b >= 2:
                        pe.wait_ge(S["ouT_copied"], b - 1)
                    transpose_batch(bank[4 + b % 2], XN[:, b, :], "ouT_done")
                if s >= 1:
                    b = s - 1
                    pe.wait_ge(S["ouT_copied"], b + 1)
                    if b >= 2:
                        pe.wait_ge(S["y_biased"], b - 1)
                    project(bank[6 + b % 2], XT[:, b % 2, :], [w_out[:, k, :] for k in range(KC)], "wo_done")

            pe.wait_ge(S["gate_loaded"], 16)
            for s in range(B + 1):
                if s < B:
                    b = s
                    pe.wait_ge(S["xn2_done"], J * (b + 1))
                    if b >= 2:
                        pe.wait_ge(S["xn2T_copied"], b - 1)
                    transpose_batch(bank[b % 2], V[:, b, :], "xn2T_done")
                if s >= 1:
                    b = s - 1
                    pe.wait_ge(S["xn2T_copied"], b + 1)
                    for j in range(J):
                        i = b * J + j
                        for k in range(KC):
                            last = pe.matmul(bank[2][:, i * E:(i + 1) * E], chunk(QT[:, b, :], k, j),
                                             gate_w[:, k, :], start=(k == 0), stop=(k == KC - 1))
                    last.then_inc(S["logits_done"], 1)

            pe.wait_ge(S["mask_done"], 1)
            pe.wait_ge(S["const_done"], 9)
            m = mask[:, :, :].rearrange("p t e -> p (t e)")
            pe.matmul(bank[3][:, 0:T * E], before[:, :], m, start=True, stop=False, skip_group_check=True)
            for d in range(1, T):
                last = pe.matmul(bank[3][:, d * E:T * E], ones[:, :], m[:, 0:(T - d) * E], start=False,
                                 stop=(d == T - 1), skip_group_check=True)
            last.then_inc(S["prefix_done"], 1)
            for i in range(T):
                last = pe.matmul(bank[4][:, 0:E], ones[:, :], m[:, i * E:(i + 1) * E], start=(i == 0),
                                 stop=(i == T - 1))
            last.then_inc(S["counts_done"], 1)
            pe.wait_ge(S["vals_done"], 1)
            n = 0
            for e in range(E):
                for i in range(T):
                    pe.wait_ge(S["sel_done"], n + 1)
                    last = pe.matmul(bank[5][:, e * 3 * RT:(e + 1) * 3 * RT], sel[:, n % 4, :],
                                     vals[:, i, e, :, :].rearrange("p q r -> p (q r)"),
                                     start=(i == 0), stop=(i == T - 1)).then_inc(S["sel_used"], 1)
                    n += 1
            pe.wait_ge(S["sel_used"], n)
            pe.matmul(bank[6][:, 0:1], ident[:, :], ident[:, 0:1], start=True, stop=True).then_inc(S["inv_mm"], 1)

            def x_transpose(t):
                pe.wait_ge(S["gathered"], (t + 1) * 16)
                if not first(t):
                    pe.wait_ge(S["t_lo"], t)
                for k in range(KC):
                    last = pe.transpose(bank[3][:, k * P:(k + 1) * P], x_tile[:, k * P:(k + 1) * P], ident[:, :])
                last.then_inc(S["tT_done"], 1)

            def up_or_gate(which, ring, done):
                ps = bank[0 if which else 1][:, 0:HID]

                def w(t, k):
                    return t[:, ring, (which * KC + k) * HID:(which * KC + k + 1) * HID]

                for k in range(KC):
                    pe.matmul(ps, x_hi[:, k, :], w(ug_hi, k), start=(k == 0), stop=False)
                    pe.matmul(ps, x_hi[:, k, :], w(ug_lo, k), start=False, stop=False)
                if which:
                    pe.wait_ge(S["t_lo"], done)
                for k in range(KC):
                    last = pe.matmul(ps, x_lo[:, k, :], w(ug_hi, k), start=False, stop=(k == KC - 1))
                last.then_inc(S["gate_done" if which else "up_done"], 1)

            def expert_of(t):
                e = pe.value_load(tab_e[0:1, bass.ds(t, 1)], min_val=0, max_val=E - 1)
                ring = pe.value_load(tab_slot[0:1, bass.ds(t, 1)], min_val=0, max_val=NB_RING - 1)
                return e, ring

            def gate(t, ring):
                pe.wait_ge(S["t_hi"], t + 1)
                if not first(t):
                    pe.wait_ge(S["silu_done"], t)
                up_or_gate(1, ring, t + 1)

            def up(t, ring):
                if not first(t):
                    pe.wait_ge(S["h_done"], t)
                up_or_gate(0, ring, t + 1)

            def h_transpose(t):
                pe.wait_ge(S["h_done"], t + 1)
                if not first(t):
                    pe.wait_ge(S["hT_lo"], t)
                for k in range(HC):
                    last = pe.transpose(bank[2][0:HP, k * P:(k + 1) * P], h_tile[:, k * HP:(k + 1) * HP],
                                        ident[:, :])
                last.then_inc(S["hT_done"], 1)

            def down(t, ring):
                pe.wait_ge(S["hT_hi"], t + 1)
                if not first(t):
                    pe.wait_ge(S["y_ready"], t)
                ps = bank[4][:, 0:C]

                def w(t, k):
                    return t[:, ring, k * C:(k + 1) * C]

                for k in range(HC):
                    pe.matmul(ps, h_hi[:, k, :], w(dn_hi, k), start=(k == 0), stop=False)
                    pe.matmul(ps, h_hi[:, k, :], w(dn_lo, k), start=False, stop=False)
                pe.wait_ge(S["hT_lo"], t + 1)
                for k in range(HC):
                    last = pe.matmul(ps, h_lo[:, k, :], w(dn_hi, k), start=False, stop=(k == HC - 1))
                last.then_inc(S["down_done"], 1)

            pe.wait_ge(S["tables_done"], 1)
            pe.wait_ge(S["inv_done"], 1)
            x_transpose(0)
            pe.wait_ge(S["lo_split"], 2)
            gate(0, 0)
            up(0, 0)
            x_transpose(1)

            def step(t):
                e, ring = expert_of(t + 1)
                ring_now = pe.value_load(tab_slot[0:1, bass.ds(t, 1)], min_val=0, max_val=NB_RING - 1)
                pe.wait_ge(S["lo_split"], 2 * e + 2)
                gate(t + 1, ring)
                h_transpose(t)
                up(t + 1, ring)
                x_transpose(t + 2)
                down(t, ring_now)

            step(0)
            with pe.Fori(1, NT - 2, 1) as t:
                step(t)
            h_transpose(NT - 2)
            last_ring = pe.value_load(tab_slot[0:1, NT - 2:NT - 1], min_val=0, max_val=NB_RING - 1)
            down(NT - 2, last_ring)


def kernel(**inputs):
    import numpy as _np
    import concourse.bacc as _bacc
    from concourse import mybir as _mybir
    from concourse.bass_utils import run_bass_kernel_spmd as _run

    P, KC, HC = 128, 2, 4
    up, gate, down = (_np.asarray(inputs["L0_ffn_" + n]) for n in ("W_up", "W_gate", "W_down"))
    E, H, C = up.shape

    def by_channel(w):
        return w.transpose(0, 2, 1).reshape(E, KC, P, H).transpose(0, 2, 1, 3)

    named = {n: inputs["L0_attn_" + n] for n in
             ("x", "Wqk", "bqk", "Wv", "bv", "Wu", "bu", "Wo", "bo", "ln_g", "ln_b")}
    named["w_ug"] = _np.concatenate([by_channel(up), by_channel(gate)], axis=2).reshape(E, P, 2 * KC * H)
    named["w_dn"] = down.transpose(0, 2, 1).reshape(E, HC, H // HC, C).transpose(0, 2, 1, 3).reshape(
        E, H // HC, HC * C)
    named["gate_t"] = _np.asarray(inputs["L0_ffn_gate_inp"]).T

    nc = _bacc.Bacc("TRN2", target_bir_lowering=False, num_devices=1)
    arrays, args = {}, []
    for name, a in named.items():
        a = _np.ascontiguousarray(a)
        arrays[f"in_{name}_dram"] = a
        args.append(nc.dram_tensor(f"in_{name}_dram", a.shape, _mybir.dt.from_np(a.dtype), kind="ExternalInput").ap())
    shape = named["x"].shape
    args.append(nc.dram_tensor("out_0_dram", shape, F32, kind="ExternalOutput").ap())
    sandwich_kernel(nc, *args)
    r = _run(nc, [arrays], core_ids=[0])
    return r.results[0]["out_0_dram"]
```
